# Optimizing a Trainium2 kernel written in Bass

```python
import numpy as np
import jax
import jax.numpy as jnp

def _softmax(x, axis=-1):
    return jax.nn.softmax(x, axis=axis)

def _gelu(x):
    return jax.nn.gelu(x, approximate=True)

def _silu(x):
    return jax.nn.silu(x)

def _sigmoid(x):
    return jax.nn.sigmoid(x)

def _layernorm(x, axis=-1, eps=1e-05):
    m = jnp.mean(x, axis=axis, keepdims=True)
    v = jnp.var(x, axis=axis, keepdims=True)
    return (x - m) / jnp.sqrt(v + eps)

def _scatter_add(tgt, idx, src, axis=0):
    return tgt.at[idx].add(src)

def _segment_sum(src, seg, n):
    return jax.ops.segment_sum(src, seg, n)
kernel_name = 'mk_xattn_ffn_d1_seqx_r4_f09b31'

def setup_inputs(seed: int=0):
    np.random.seed(seed)
    _w = jnp.asarray

    def _rec_inputs():
        import jax
        import jax.numpy as jnp
        _rk = jax.random.key(seed)
        x = -0.000125 + 0.9999 * jax.random.normal(jax.random.fold_in(_rk, 1), (32, 128, 1024), jnp.float32)
        _lenS = 128 - jax.random.randint(jax.random.fold_in(_rk, 7), (32,), 0, max(1, 128 // 4) + 1, jnp.int32)
        _lenS2 = 128 - jax.random.randint(jax.random.fold_in(_rk, 8), (32,), 0, max(1, 128 // 4) + 1, jnp.int32)
        _ctx_4096P = jax.random.normal(jax.random.fold_in(_rk, 11), (32, 16, 1024), jnp.float32)
        _ctx_4096c = jax.random.dirichlet(jax.random.fold_in(_rk, 511), 0.3 * jnp.ones((16,), jnp.float32), (32, 128))
        _ctx_4096t = jnp.einsum('bsk,bkd->bsd', _ctx_4096c, _ctx_4096P)
        _ctx_4096t = _ctx_4096t * jax.lax.rsqrt(jnp.mean(jnp.square(_ctx_4096t)) + 1e-12) * 0.953939
        ctx_4096 = -1.52775e-05 + 0.999936 * (_ctx_4096t + 0.3 * jax.random.normal(jax.random.fold_in(_rk, 611), (32, 128, 1024), jnp.float32))
        return (x, ctx_4096)
    x, ctx_4096 = _rec_inputs()

    def _L0_xattn_setup():
        import jax, jax.numpy as jnp
        import numpy as np
        H = 8
        C = 2

        def _autocorrelation(Q, K, V):
            B, L, D = Q.shape
            d = D // H
            q = Q.reshape(B, L, H, d).transpose(0, 2, 1, 3)
            k = K.reshape(B, L, H, d).transpose(0, 2, 1, 3)
            v = V.reshape(B, L, H, d).transpose(0, 2, 1, 3)
            qf = jnp.fft.fft(q, axis=2)
            kf = jnp.fft.fft(k, axis=2)
            corr = jnp.fft.ifft(qf * jnp.conj(kf), axis=2).real
            topk = int(C * np.log(L))
            w, idx = jax.lax.top_k(corr.transpose(0, 1, 3, 2), topk)
            w = jax.nn.softmax(w, axis=-1)
            pos = jnp.arange(L)[:, None]
            out = jnp.zeros_like(v)
            for i in range(topk):
                g = jnp.minimum(idx[:, :, None, :, i] + pos, L - 1)
                out = out + w[:, :, None, :, i] * jnp.take_along_axis(v, g, axis=2)
            return out.transpose(0, 2, 1, 3).reshape(B, L, D)
        key = jax.random.key(seed)
        k1, k2, k3 = jax.random.split(key, 3)
        B, L, D = (16, 128, 1024)
        Q = jax.random.normal(k1, (B, L, D), dtype=jnp.float32)
        K = jax.random.normal(k2, (B, L, D), dtype=jnp.float32)
        V = jax.random.normal(k3, (B, L, D), dtype=jnp.float32)
        return {'Q': Q, 'K': K, 'V': V}
    _L0_xattn_all = _L0_xattn_setup()
    _L0_xattn_in = {k: v for k, v in _L0_xattn_all.items() if k in ()}
    del _L0_xattn_all

    def _L0_ffn_setup():
        import jax, jax.numpy as jnp
        import numpy as np
        BATCH, SEQ, D = (2, 512, 1024)
        K, TOPK, RANK = (64, 16, 16)
        ALPHA = 32.0
        SCALING = ALPHA / RANK
        key = jax.random.key(seed)
        k1, k2, k3, k4 = jax.random.split(key, 4)
        x = jax.random.normal(k1, (BATCH, SEQ, D), dtype=jnp.float32)
        A = jax.random.normal(k2, (K, RANK, D), dtype=jnp.float32) * 0.02
        B = jax.random.normal(k3, (K, D, RANK), dtype=jnp.float32) * 0.02
        Wr = jax.random.normal(k4, (K, D), dtype=jnp.float32) * 0.02
        return {'x': x, 'A': A, 'B': B, 'Wr': Wr}
    _L0_ffn_all = _L0_ffn_setup()
    _L0_ffn_in = {k: v for k, v in _L0_ffn_all.items() if k in ('A', 'B', 'Wr')}
    del _L0_ffn_all
    return {'x': x, 'ctx_4096': ctx_4096, 'L0_ffn_A': _L0_ffn_in['A'], 'L0_ffn_B': _L0_ffn_in['B'], 'L0_ffn_Wr': _L0_ffn_in['Wr']}

def reference(x, ctx_4096, L0_ffn_A, L0_ffn_B, L0_ffn_Wr):
    import jax
    import jax.numpy as jnp

    def _L0_xattn_ref(Q, K, V):
        import jax, jax.numpy as jnp
        import numpy as np
        H = 8
        C = 2

        def _autocorrelation(Q, K, V):
            B, L, D = Q.shape
            d = D // H
            q = Q.reshape(B, L, H, d).transpose(0, 2, 1, 3)
            k = K.reshape(B, L, H, d).transpose(0, 2, 1, 3)
            v = V.reshape(B, L, H, d).transpose(0, 2, 1, 3)
            qf = jnp.fft.fft(q, axis=2)
            kf = jnp.fft.fft(k, axis=2)
            corr = jnp.fft.ifft(qf * jnp.conj(kf), axis=2).real
            topk = int(C * np.log(L))
            w, idx = jax.lax.top_k(corr.transpose(0, 1, 3, 2), topk)
            w = jax.nn.softmax(w, axis=-1)
            pos = jnp.arange(L)[:, None]
            out = jnp.zeros_like(v)
            for i in range(topk):
                g = jnp.minimum(idx[:, :, None, :, i] + pos, L - 1)
                out = out + w[:, :, None, :, i] * jnp.take_along_axis(v, g, axis=2)
            return out.transpose(0, 2, 1, 3).reshape(B, L, D)
        return _autocorrelation(Q, K, V)

    def _L0_ffn_ref(x, A, B, Wr):
        import jax, jax.numpy as jnp
        import numpy as np
        BATCH, SEQ, D = (2, 512, 1024)
        K, TOPK, RANK = (64, 16, 16)
        ALPHA = 32.0
        SCALING = ALPHA / RANK
        prefix = x.shape[:-1]
        xf = x.reshape(-1, x.shape[-1])
        N = xf.shape[0]
        scores = xf @ Wr.T
        top_vals, top_idx = jax.lax.top_k(scores, TOPK)
        gates = jax.nn.softmax(top_vals, axis=-1)
        G = jnp.zeros((N, K), xf.dtype).at[jnp.arange(N)[:, None], top_idx].set(gates)
        h = jnp.einsum('nd,krd->nkr', xf, A)
        out = jnp.einsum('nkr,kdr->nd', h * G[:, :, None], B)
        return (out * SCALING).reshape(*prefix, -1)
    x = x + _L0_xattn_ref(_layernorm(x, axis=-1), ctx_4096, ctx_4096)
    x = x + _L0_ffn_ref(_layernorm(x, axis=-1), L0_ffn_A, L0_ffn_B, L0_ffn_Wr)
    return x

_drawn_inputs = setup_inputs


def setup_inputs(seed=0):
    import zlib

    import numpy as np

    out = dict(_drawn_inputs(seed))
    spreads = {}
    factors = {'L0_ffn_A': 2.723, 'L0_ffn_Wr': 2.978}
    for name, (base, spread) in spreads.items():
        noise = np.random.default_rng([zlib.crc32(name.encode()), seed]).standard_normal(out[name].shape)
        drawn = base * np.exp(spread * noise) if base else spread * noise
        out[name] = jnp.asarray(drawn.astype(out[name].dtype))
    for name, factor in factors.items():
        out[name] = (out[name] * factor).astype(out[name].dtype)
    return out
```

```python
import concourse.bass as bass
from concourse import mybir
from contextlib import ExitStack
import numpy as np

L = 128
D = 1024
ROWS = 32
CH = 512
NT = CH // L
HALF = L // 2
TOPK = int(2 * np.log(L))
assert TOPK == 9
EXPERTS, RANK, CHOSEN = 64, 16, 16
KR_ALL = EXPERTS * RANK
SCALING = 32.0 / RANK
NC = D // L
AWC = KR_ALL + EXPERTS
GROUPS = ((0, 512), (512, 800), (800, AWC))
LN_EPS = 1e-5
TAKEN = -3.0e38

PLAIN = ("ident", "corr_inv")
SPLIT = ("even_fwd", "even_fwd_v", "odd_fwd", "odd_fwd_v", "even_inv", "odd_inv")


def constant_matrices():
    t = np.arange(L)
    k = np.arange(1, HALF)
    even = np.zeros((L, L))
    even[:, 0] = 1.0
    even[:, 1:HALF] = np.cos(2 * np.pi * np.outer(t, k) / L)
    even[:, HALF] = np.where(t % 2 == 0, 1.0, -1.0)
    even[:, HALF + 1:] = -np.sin(2 * np.pi * np.outer(t, k) / L)
    even_v = even.copy()
    even_v[L - 1, 0] += L
    theta = np.pi * (2 * np.arange(HALF) + 1) / L
    odd = np.concatenate([np.cos(np.outer(t, theta)), -np.sin(np.outer(t, theta))], 1)
    odd_v = odd.copy()
    odd_v[L - 1] -= odd.sum(0)
    inv = even.T * (2.0 / L)
    inv[0] /= 2
    inv[HALF] /= 2
    even_inv = inv / 2
    even_inv[HALF + 1:] *= -1
    odd_inv = odd.T / L
    odd_inv[HALF:] *= -1
    return dict(ident=np.eye(L), corr_inv=inv, even_fwd=even, even_fwd_v=even_v, odd_fwd=odd,
                odd_fwd_v=odd_v, even_inv=even_inv, odd_inv=odd_inv)


def high_part(a):
    f, e = np.frexp(a)
    return np.ldexp(np.rint(np.ldexp(f, 12)), e - 12)


def constant_arrays():
    m = constant_matrices()
    plain = np.concatenate([m[n] for n in PLAIN], 1).astype(np.float32)
    parts = []
    for n in SPLIT:
        hi = high_part(m[n])
        parts += [hi, high_part(m[n] - hi)]
    sign = np.where(np.arange(L) < HALF, 1.0, -1.0).astype(np.float32)[:, None]
    return plain, np.concatenate(parts, 1).astype(np.float32), sign


def build(nc: bass.Bass, x, ctx, a_t, wr_t, b_t, plain_c, split_c, sign_c, out):
    fp32 = mybir.dt.float32
    fp32r = mybir.dt.float32r
    ALU = mybir.AluOpType
    ACT = mybir.ActivationFunctionType

    stack = ExitStack()
    with stack:
        def sb(name, shape, dt=fp32):
            return stack.enter_context(nc.sbuf_tensor(name, shape, dt))

        def sem(name):
            return stack.enter_context(nc.semaphore(name))

        aw = [sb(f"aw_{p}", [L, NC, AWC], fp32r) for p in ("hi", "lo")]
        bt = [sb(f"bt_{p}", [L, NC, D], fp32r) for p in ("hi", "lo")]
        plain = sb("plain", [L, len(PLAIN), L])
        split = sb("split", [L, 2 * len(SPLIT), L], fp32r)
        sign = sb("sign", [L, 1])
        ident = plain[:, 0, :]
        corr_inv = plain[:, 1, :]

        def const(name):
            n = 2 * SPLIT.index(name)
            return split[:, n, :], split[:, n + 1, :]

        xa = sb("xa", [L, 2, D])
        c32 = sb("c32", [L, 2, CH])
        c_op = [sb(f"c_{p}", [L, CH], fp32r) for p in ("hi", "lo")]
        q_op = [sb(f"q_{p}", [L, CH], fp32r) for p in ("hi", "lo")]
        qf = sb("qf", [L, CH])
        qs = sb("qs", [L, CH])
        ke_r = sb("ke_r", [L, 2, CH])
        ke_i = sb("ke_i", [L, 2, CH])
        ko_r = sb("ko_r", [L, CH])
        ko_i = sb("ko_i", [L, CH])
        rest = sb("rest", [L, NT, L])
        w = sb("w", [L, NT, L])
        wt_op = [sb(f"wt_{p}", [L, CH], fp32r) for p in ("hi", "lo")]
        ze_op = wt_op
        zo_op = [sb(f"zo_{p}", [L, CH], fp32r) for p in ("hi", "lo")]
        we = sb("we", [L, CH])
        we_s = sb("we_s", [L, CH])
        wo = sb("wo", [L, CH])
        wo_s = sb("wo_s", [L, CH])
        res = sb("res", [L, 2, D])
        act_in = sb("act_in", [L, D])
        t_op = [sb(f"t_{p}", [L, NC, L], fp32r) for p in ("hi", "lo")]
        top8 = sb("top8", [L, NT, 8])
        neg_max = sb("neg_max", [L, NT])
        next8 = sb("next8", [L, NT, 8])
        ninth = sb("ninth", [L, NT, 8])
        w_sum = sb("w_sum", [L, NT])
        w_inv = sb("w_inv", [L, NT])
        stats = sb("stats", [L, 2, 2, 6])
        mv = sb("mv", [L, 2, 2])
        rstd = sb("rstd", [L, 2])
        shift = sb("shift", [L, 2])
        minus_half = sb("minus_half", [L, 1])
        g8a = sb("g8a", [L, 8])
        g8b = sb("g8b", [L, 8])
        g_neg = sb("g_neg", [L, 1])
        g_rest = sb("g_rest", [L, EXPERTS])
        g_mark = sb("g_mark", [L, EXPERTS])
        g_exp = sb("g_exp", [L, EXPERTS])
        gate = sb("gate", [L, EXPERTS])
        g_sum = sb("g_sum", [L, 1])
        g_inv = sb("g_inv", [L, 1])
        out_scale = sb("out_scale", [L, 1])

        bank = [stack.enter_context(nc.psum_tensor(f"bank{b}", [L, 512], fp32)) for b in range(8)]
        P_H = bank[0:3]
        P_Y = bank[0:2]
        P_T = bank[3:5]
        P_KO = bank[3]
        P_WT = P_WE = bank[5]
        P_Q = P_WO = P_OUT = bank[6]
        P_KE = P_CORR = bank[7]

        stage = [act_in[:, 0:CH], act_in[:, CH:], res[:, 1, 0:CH], res[:, 1, CH:]]
        split_flat = split[:, :, :].rearrange("p n l -> p (n l)")
        jobs = [(split_c[:, n:n + CH], split_flat[:, n:n + CH], None) for n in range(0, 2 * len(SPLIT) * L, CH)]
        CONSTANTS = len(jobs)
        jobs += [(wr_t.rearrange("(c p) e -> p c e", p=L), aw[0][:, :, KR_ALL:], aw[1][:, :, KR_ALL:])]
        for src, dst in ((a_t, aw), (b_t, bt)):
            jobs += [(src[c * L:(c + 1) * L, n:n + CH], dst[0][:, c, n:n + CH], dst[1][:, c, n:n + CH])
                     for c in range(NC) for n in (0, CH)]
        PER_SLOT = -(-(len(jobs) - CONSTANTS) // 4)

        def staged(n):
            v = stage[n % 4]
            return v.rearrange("p (c e) -> p c e", e=EXPERTS) if n == CONSTANTS else v

        def jobs_of(i, s):
            first = CONSTANTS + (2 * i + s) * PER_SLOT
            return range(first, min(first + PER_SLOT, len(jobs)))

        const_in = sem("const_in")
        staged_in = [sem(f"staged_in{n}") for n in range(4)]
        x_in = [sem(f"x_in{p}") for p in range(2)]
        c_in = [sem(f"c_in{p}") for p in range(2)]
        q_swapped, ke_doubled, ko_doubled = sem("q_swapped"), sem("ke_doubled"), sem("ko_doubled")
        we_swapped, wo_swapped = sem("we_swapped"), sem("wo_swapped")
        stored = [sem(f"stored{p}") for p in range(2)]
        zeroed = sem("zeroed")
        q_lo, c_lo, q_terms, e_terms, o_terms = (sem(n) for n in ("q_lo", "c_lo", "q_terms", "e_terms", "o_terms"))
        ze_lo, zo_lo, w_ready, half_kept = (sem(n) for n in ("ze_lo", "zo_lo", "w_ready", "half_kept"))
        ln1, ln2, rstd1, rstd2 = (sem(n) for n in ("ln1", "ln2", "rstd1", "rstd2"))
        hi_staged = sem("hi_staged")
        q_hi, q_full, c_hi, wt_hi, q_out, ke_out, ko_out = (
            sem(n) for n in ("q_hi", "q_full", "c_hi", "wt_hi", "q_out", "ke_out", "ko_out"))
        t_hi, we_out, wo_out, ze_hi, zo_hi, w_exp, ln_out, gate_exp = (
            sem(n) for n in ("t_hi", "we_out", "wo_out", "ze_hi", "zo_hi", "w_exp", "ln_out", "gate_exp"))
        lo_staged = sem("lo_staged")
        mv1, mv2, wt_lo, t_lo, zc, ze, zo, marked8, w_summed, x2 = (
            sem(n) for n in ("mv1", "mv2", "wt_lo", "t_lo", "zc", "ze", "zo", "marked8", "w_summed", "x2"))
        real_term, real_terms = sem("real_term"), sem("real_terms")
        gates_marked, gated, result = (sem(n) for n in ("gates_marked", "gated", "result"))
        ln1_step, ln2_step, top_step, gate_step = (sem(n) for n in ("ln1_step", "ln2_step", "top_step", "gate_step"))
        wt_mm, q_mm, ke_mm, t_mm, we_mm, wo_mm, corr_mm, ko_mm, out_mm, h_mm, y_mm = (
            sem(n) for n in ("wt_mm", "q_mm", "ke_mm", "t_mm", "we_mm", "wo_mm", "corr_mm", "ko_mm", "out_mm",
                             "h_mm", "y_mm"))

        def after(eng, s, n):
            if not (isinstance(n, int) and n <= 0):
                eng.wait_ge(s, n)

        def alone(eng, s, n):
            if isinstance(n, int):
                eng.wait_ge(s, n)
                return
            with eng.register() as count:
                eng.reg_mov(count, n)
                n = eng.snap(count, min_val=1)
                eng.wait_ge(const_in, 32)
                eng.wait_ge(s, n)

        def iterations(eng, body):
            def peeled(i):
                body(i // 2, i % 2, i < ROWS, 1 <= i <= ROWS, i >= 2, i + 1 < ROWS)
            for i in (0, 1):
                peeled(i)
            with eng.Fori(1, ROWS // 2 - 1) as m:
                body(m, 0, True, True, True, True)
                body(m, 1, True, True, True, True)
            for i in range(ROWS - 2, ROWS + 2):
                peeled(i)

        block = stack.enter_context(nc.Block())

        @block.sync
        def _(sp):
            sp.dma_start(plain[:, :, :], plain_c.rearrange("p (n l) -> p n l", l=L)).then_inc(const_in, 16)
            sp.dma_start(sign[:, :], sign_c).then_inc(const_in, 16)

            def stage_in(n):
                if n >= 4:
                    sp.wait_ge(hi_staged, n - 3)
                    after(sp, lo_staged, n - 3 - CONSTANTS)
                sp.dma_start(staged(n), jobs[n][0]).then_inc(staged_in[n % 4], 16)

            def load_x(row, k):
                sp.dma_start(xa[:, k, :], x[bass.ds(row, 1), :, :].rearrange("a p d -> (a p) d")).then_inc(x_in[k], 16)

            def load_c(row, s):
                sp.dma_start(c32[:, s, :], ctx[bass.ds(row, 1), :, s * CH:(s + 1) * CH]
                             .rearrange("a p d -> (a p) d")).then_inc(c_in[s], 16)

            load_x(0, 0)
            load_c(0, 0)
            for n in range(CONSTANTS):
                stage_in(n)
            load_c(0, 1)

            def body(m, k, att, back, ffn, more):
                i = 2 * m + k
                if isinstance(m, int):
                    next_row, done_row = i + 1, i - 2
                else:
                    next_row, done_row = sp.snap(i + 1), sp.snap(i - 2)
                for s in range(2):
                    u = 2 * i + s
                    v = u - 1
                    if s == 1 and more:
                        after(sp, x2, 2 * i)
                        after(sp, half_kept, i)
                        load_x(next_row, 1 - k)
                    if att:
                        sp.wait_ge(q_out, u + 1)
                        after(sp, zc, u)
                        sp.dma_start(qs[1:HALF, :], qf[HALF + 1:L, :]).then_inc(q_swapped, 16)
                        sp.dma_start(qs[HALF + 1:L, :], qf[1:HALF, :]).then_inc(q_swapped, 16)
                        sp.wait_ge(ke_out, u + 1)
                        sp.dma_start(ke_r[HALF + 1:L, s, :], ke_r[1:HALF, s, :]).then_inc(ke_doubled, 16)
                        sp.dma_start(ke_i[1:HALF, s, :], ke_i[HALF + 1:L, s, :]).then_inc(ke_doubled, 16)
                    if (back if s == 0 else att):
                        after(sp, ze, v)
                        sp.wait_ge(we_out, v + 1)
                        sp.dma_start(we_s[1:HALF, :], we[HALF + 1:L, :]).then_inc(we_swapped, 16)
                        sp.dma_start(we_s[HALF + 1:L, :], we[1:HALF, :]).then_inc(we_swapped, 16)
                        sp.wait_ge(wo_out, v + 1)
                        after(sp, zo, v)
                        sp.dma_start(wo_s[0:HALF, :], wo[HALF:L, :]).then_inc(wo_swapped, 16)
                        sp.dma_start(wo_s[HALF:L, :], wo[0:HALF, :]).then_inc(wo_swapped, 16)
                    if att and more:
                        sp.wait_ge(c_hi, u + 1)
                        sp.wait_ge(c_lo, u + 1)
                        load_c(next_row, s)
                    if att:
                        sp.wait_ge(ko_out, u + 1)
                        sp.dma_start(ko_r[HALF:L, :], ko_r[0:HALF, :]).then_inc(ko_doubled, 16)
                        sp.dma_start(ko_i[0:HALF, :], ko_i[HALF:L, :]).then_inc(ko_doubled, 16)
                    if isinstance(m, int) and i < 2:
                        for n in jobs_of(i, s):
                            stage_in(n)
                    if s == 1 and ffn:
                        sp.wait_ge(result, 2 * (i - 1))
                        sp.dma_start(out[bass.ds(done_row, 1), :, :].rearrange("a p d -> (a p) d"),
                                     res[:, k, :]).then_inc(stored[k], 16)

            iterations(sp, body)
            for k in range(2):
                sp.wait_ge(stored[k], 16 * (ROWS // 2))

        @block.tensor
        def _(pe):
            def three(dst, st, mv_, start, stop):
                nc.tensor.matmul(dst, st[0], mv_[0], start=start, stop=False)
                nc.tensor.matmul(dst, st[0], mv_[1], start=False, stop=False)
                return nc.tensor.matmul(dst, st[1], mv_[0], start=False, stop=stop)

            def pair(t):
                return t[0][:, :], t[1][:, :]

            def transposes():
                for h in range(2):
                    for c in range(NC // 2):
                        last = nc.tensor.transpose(P_T[h][:, c * L:(c + 1) * L],
                                                   act_in[:, (4 * h + c) * L:(4 * h + c + 1) * L], ident)
                    last.then_inc(t_mm, 1)

            def h_group(g, j):
                lo, hi = GROUPS[g]
                for c in range(NC):
                    if g == 2 and c % 4 == 0:
                        pe.wait_ge(t_hi, 4 * j + c // 4 + 1)
                        pe.wait_ge(t_lo, 4 * j + c // 4 + 1)
                    last = three(P_H[g][:, 0:hi - lo], (t_op[0][:, c, :], t_op[1][:, c, :]),
                                 (aw[0][:, c, lo:hi], aw[1][:, c, lo:hi]), c == 0, c == NC - 1)
                last.then_inc(h_mm, 1)

            def y_half(h, j):
                for c in range(NC):
                    if h == 0 and c % 4 == 0:
                        pe.wait_ge(t_hi, 4 * j + c // 4 + 3)
                        pe.wait_ge(t_lo, 4 * j + c // 4 + 3)
                    last = three(P_Y[h][:, :], (t_op[0][:, c, :], t_op[1][:, c, :]),
                                 (bt[0][:, c, h * 512:(h + 1) * 512], bt[1][:, c, h * 512:(h + 1) * 512]),
                                 c == 0, c == NC - 1)
                last.then_inc(y_mm, 1)

            pe.wait_ge(const_in, 32)
            pe.wait_ge(hi_staged, CONSTANTS)

            def body(m, k, att, back, ffn, more):
                i = 2 * m + k
                j = i - 2
                if isinstance(m, int) and i == 2:
                    pe.wait_ge(hi_staged, len(jobs))
                    pe.wait_ge(lo_staged, len(jobs) - CONSTANTS)
                for s in range(2):
                    u = 2 * i + s
                    v = u - 1
                    prev = back if s == 0 else att
                    if ffn:
                        if s == 0:
                            pe.wait_ge(ln_out, j + 1)
                        else:
                            pe.wait_ge(gated, 3 * (j + 1))
                        after(pe, ko_out, u if att else 2 * ROWS)
                        transposes()
                    if prev:
                        pe.wait_ge(w_ready, v + 1)
                        after(pe, we_out, v)
                        for t in range(NT):
                            last = nc.tensor.transpose(P_WT[:, t * L:(t + 1) * L], w[:, t, :], ident)
                        last.then_inc(wt_mm, 1)
                    if att:
                        pe.wait_ge(q_hi, u + 1)
                        pe.wait_ge(q_lo, u + 1)
                        after(pe, x2, v)
                        three(P_Q[:, :], const("even_fwd"), pair(q_op), True, True).then_inc(q_mm, 1)
                        pe.wait_ge(c_hi, u + 1)
                        pe.wait_ge(c_lo, u + 1)
                        three(P_KE[:, :], const("even_fwd_v"), pair(c_op), True, True).then_inc(ke_mm, 1)
                    if prev:
                        pe.wait_ge(wt_hi, v + 1)
                        pe.wait_ge(wt_lo, v + 1)
                        three(P_WE[:, :], const("even_fwd"), pair(wt_op), True, True).then_inc(we_mm, 1)
                        if att:
                            pe.wait_ge(q_out, u + 1)
                        else:
                            pe.wait_ge(x2, v)
                        three(P_WO[:, :], const("odd_fwd"), pair(wt_op), True, True).then_inc(wo_mm, 1)
                    if ffn and s == 0:
                        after(pe, result, 2 * j)
                        h_group(2, j)
                        h_group(1, j)
                    if ffn and s == 1:
                        y_half(0, j)
                    if att:
                        pe.wait_ge(zc, u + 1)
                        pe.wait_ge(ke_out, u + 1)
                        for t in range(NT):
                            last = nc.tensor.matmul(P_CORR[:, t * L:(t + 1) * L], qf[:, t * L:(t + 1) * L], corr_inv,
                                                    start=True, stop=True)
                        last.then_inc(corr_mm, 1)
                        if not ffn:
                            after(pe, ko_out, u)
                        three(P_KO[:, :], const("odd_fwd_v"), pair(c_op), True, True).then_inc(ko_mm, 1)
                    if ffn and s == 0:
                        h_group(0, j)
                    if ffn and s == 1:
                        y_half(1, j)
                    if prev:
                        pe.wait_ge(ze_hi, v + 1)
                        pe.wait_ge(ze_lo, v + 1)
                        pe.wait_ge(zo_hi, v + 1)
                        pe.wait_ge(zo_lo, v + 1)
                        pe.wait_ge(wo_out, v + 1)
                        three(P_OUT[:, :], const("even_inv"), pair(ze_op), True, False)
                        three(P_OUT[:, :], const("odd_inv"), pair(zo_op), False, True).then_inc(out_mm, 1)

            iterations(pe, body)

        @block.scalar
        def _(act):
            def copy(dst, src):
                return nc.scalar.activation(dst, src, ACT.Copy)

            def norm(dst, src, n):
                return nc.scalar.activation(dst, src, ACT.Identity, bias=shift[:, n:n + 1], scale=rstd[:, n:n + 1])

            def split_c_hi(u, s, i):
                act.wait_ge(c_in[s], 16 * (i + 1))
                after(act, ko_mm, u)
                copy(c_op[0][:, :], c32[:, s, :]).then_inc(c_hi, 1)

            def split_q_hi(u, s, i, k):
                act.wait_ge(ln1, i + 1)
                after(act, corr_mm, u)
                xs = xa[:, k, s * CH:(s + 1) * CH]
                norm(qf[:, :], xs, 0).then_inc(q_full, 1)
                norm(q_op[0][:, :], xs, 0).then_inc(q_hi, 1)

            def stage_hi(n):
                act.wait_ge(staged_in[n % 4], 16 * (n // 4 + 1))
                copy(jobs[n][1], staged(n)).then_inc(hi_staged, 1)

            for n in range(CONSTANTS):
                stage_hi(n)
            split_c_hi(0, 0, 0)
            split_q_hi(0, 0, 0, 0)

            def body(m, k, att, back, ffn, more):
                i = 2 * m + k
                j = i - 2
                for s in range(2):
                    u = 2 * i + s
                    v = u - 1
                    prev = back if s == 0 else att
                    if ffn:
                        for h in range(2):
                            act.wait_ge(t_mm, 4 * j + 2 * s + h + 1)
                            if h == 0:
                                if s == 0:
                                    after(act, y_mm, 2 * j)
                                else:
                                    act.wait_ge(h_mm, 3 * (j + 1))
                            copy(t_op[0][:, 4 * h:4 * h + 4, :].rearrange("p c l -> p (c l)"), P_T[h][:, :])\
                                .then_inc(t_hi, 1)
                    if prev:
                        act.wait_ge(wt_mm, v + 1)
                        after(act, out_mm, v)
                        copy(wt_op[0][:, :], P_WT[:, :]).then_inc(wt_hi, 1)
                    if att:
                        act.wait_ge(q_mm, u + 1)
                        copy(qf[:, :], P_Q[:, :]).then_inc(q_out, 1)
                        act.wait_ge(ke_mm, u + 1)
                        after(act, ze, u - 1)
                        copy(ke_r[:, s, :], P_KE[:, :])
                        copy(ke_i[HALF:L, s, :], P_KE[HALF:L, :]).then_inc(ke_out, 1)
                    if prev:
                        act.wait_ge(we_mm, v + 1)
                        after(act, ze_lo, v)
                        copy(we[:, :], P_WE[:, :]).then_inc(we_out, 1)
                        act.wait_ge(wo_mm, v + 1)
                        after(act, zo_lo, v)
                        copy(wo[:, :], P_WO[:, :]).then_inc(wo_out, 1)
                    if s == 0 and back:
                        act.wait_ge(x2, 2 * i - 1)
                        after(act, stored[1 - k], 16 * (m + k - 1))
                        copy(res[:, 1 - k, 0:CH], xa[:, 1 - k, 0:CH]).then_inc(half_kept, 1)
                    if ffn and s == 0:
                        act.wait_ge(gates_marked, j + 1)
                        nc.scalar.activation(g_exp[:, :], P_H[2][:, GROUPS[2][1] - GROUPS[2][0] - EXPERTS:
                                                                 GROUPS[2][1] - GROUPS[2][0]],
                                             ACT.Exp, bias=g_neg[:, :]).then_inc(gate_exp, 1)
                    if prev:
                        act.wait_ge(ze, v + 1)
                        copy(ze_op[0][:, :], we[:, :]).then_inc(ze_hi, 1)
                        act.wait_ge(zo, v + 1)
                        copy(zo_op[0][:, :], wo[:, :]).then_inc(zo_hi, 1)
                    if att:
                        act.wait_ge(marked8, u + 1)
                        for t in range(NT):
                            last = nc.scalar.activation(w[:, t, :], P_CORR[:, t * L:(t + 1) * L], ACT.Exp,
                                                        bias=neg_max[:, t:t + 1])
                        last.then_inc(w_exp, 1)
                        act.wait_ge(ko_mm, u + 1)
                        after(act, zo, u)
                        copy(ko_r[:, :], P_KO[:, :])
                        copy(ko_i[HALF:L, :], P_KO[HALF:L, :]).then_inc(ko_out, 1)
                    if att and (s == 0 or more):
                        split_c_hi(u + 1, 1 - s, i + s)
                        split_q_hi(u + 1, 1 - s, i + s, k if s == 0 else 1 - k)
                    if isinstance(m, int) and i < 2:
                        for n in jobs_of(i, s):
                            stage_hi(n)
                    if s == 1 and back:
                        if isinstance(m, int) and i == 1:
                            act.wait_ge(lo_staged, len(jobs) - CONSTANTS)
                        act.wait_ge(ln2, i)
                        after(act, t_mm, 4 * (j + 1))
                        norm(act_in[:, :], res[:, 1 - k, :], 1).then_inc(ln_out, 1)

            iterations(act, body)

        @block.gpsimd
        def _(pool):
            tt = nc.gpsimd.tensor_tensor
            for t in (qs[:, :], we_s[:, :], ke_i[:, :, :]):
                nc.gpsimd.memset(t, 0.0)
            nc.gpsimd.memset(minus_half[:, :], -0.5)
            nc.gpsimd.memset(ninth[:, :, :], TAKEN).then_inc(zeroed, 1)

            def split_c_lo(u, s):
                pool.wait_ge(c_hi, u + 1)
                tt(c_op[1][:, :], c32[:, s, :], c_op[0][:, :].bitcast(fp32), ALU.subtract).then_inc(c_lo, 1)

            def split_q_lo(u):
                pool.wait_ge(q_hi, u + 1)
                tt(q_op[1][:, :], qf[:, :], q_op[0][:, :].bitcast(fp32), ALU.subtract).then_inc(q_lo, 1)

            def scale_and_shift(n, row, ready, rooted, done):
                alone(pool, ready, row + 1)
                nc.gpsimd.tensor_scalar(rstd[:, n:n + 1], mv[:, n, 1:2], LN_EPS, 1.0, ALU.add, ALU.mult)\
                    .then_inc(rooted, 1)
                pool.wait_ge(rooted, 2 * row + 1)
                tt(rstd[:, n:n + 1], rstd[:, n:n + 1], minus_half[:, :], ALU.pow).then_inc(rooted, 1)
                alone(pool, rooted, 2 * row + 2)
                nc.gpsimd.tensor_scalar(shift[:, n:n + 1], mv[:, n, 0:1], -1.0, rstd[:, n:n + 1],
                                        ALU.mult, ALU.mult).then_inc(done, 1)

            scale_and_shift(0, 0, mv1, rstd1, ln1)
            split_c_lo(0, 0)
            split_q_lo(0)

            def body(m, k, att, back, ffn, more):
                i = 2 * m + k
                j = i - 2
                for s in range(2):
                    u = 2 * i + s
                    v = u - 1
                    prev = back if s == 0 else att
                    if att:
                        pool.wait_ge(q_swapped, 32 * (u + 1))
                        pool.wait_ge(ke_doubled, 32 * (u + 1))
                        tt(qs[:, :], qs[:, :], ke_i[:, s, :], ALU.mult).then_inc(q_terms, 1)
                    if prev:
                        pool.wait_ge(we_swapped, 32 * (v + 1))
                        tt(we_s[:, :], we_s[:, :], ke_i[:, 1 - s, :], ALU.mult).then_inc(e_terms, 1)
                        pool.wait_ge(wo_swapped, 32 * (v + 1))
                        pool.wait_ge(ko_doubled, 32 * (v + 1))
                        tt(wo_s[:, :], wo_s[:, :], ko_i[:, :], ALU.mult).then_inc(o_terms, 1)
                        pool.wait_ge(ze_hi, v + 1)
                        tt(ze_op[1][:, :], we[:, :], ze_op[0][:, :].bitcast(fp32), ALU.subtract).then_inc(ze_lo, 1)
                        pool.wait_ge(zo_hi, v + 1)
                        tt(zo_op[1][:, :], wo[:, :], zo_op[0][:, :].bitcast(fp32), ALU.subtract).then_inc(zo_lo, 1)
                    if s == 1 and back:
                        after(pool, ln_out, i - 1)
                        scale_and_shift(1, i - 1, mv2, rstd2, ln2)
                    if s == 1 and more:
                        pool.wait_ge(q_hi, 2 * i + 2)
                        scale_and_shift(0, i + 1, mv1, rstd1, ln1)
                    if att and (s == 0 or more):
                        split_c_lo(u + 1, 1 - s)
                        split_q_lo(u + 1)
                    if att:
                        pool.wait_ge(w_summed, u + 1)
                        tt(w[:, :, :], w[:, :, :], w_inv[:, :, None].broadcast_to([L, NT, L]), ALU.mult)\
                            .then_inc(w_ready, 1)

            iterations(pool, body)

        @block.vector
        def _(dve):
            tt = nc.vector.tensor_tensor
            stt = nc.vector.scalar_tensor_tensor

            def statistics(src, n, row, step, done):
                for h in range(2):
                    last = nc.vector.bn_stats(stats[:, n, h, :], src[:, h * 512:(h + 1) * 512])
                last.then_inc(step, 1)
                alone(dve, step, row + 1)
                nc.vector.bn_aggr(mv[:, n, :], stats[:, n, :, :]).then_inc(done, 1)

            def choose_delays(u, corr_):
                alone(dve, corr_mm, u + 1)
                for t in range(NT):
                    last = nc.vector.max(top8[:, t, :], corr_[:, t * L:(t + 1) * L])
                last.then_inc(top_step, 1)
                dve.wait_ge(top_step, 5 * u + 1)
                nc.vector.tensor_scalar(neg_max[:, :], top8[:, :, 0], -1.0, None, ALU.mult)
                for t in range(NT):
                    last = nc.vector.match_replace(rest[:, t, :], top8[:, t, :], corr_[:, t * L:(t + 1) * L], TAKEN)
                last.then_inc(marked8, 1)
                alone(dve, marked8, u + 1)
                for t in range(NT):
                    last = nc.vector.max(next8[:, t, :], rest[:, t, :])
                last.then_inc(top_step, 1)
                dve.wait_ge(top_step, 5 * u + 2)
                nc.vector.tensor_copy(ninth[:, :, 0], next8[:, :, 0]).then_inc(top_step, 1)
                alone(dve, top_step, 5 * u + 3)
                for t in range(NT):
                    last = nc.vector.match_replace(rest[:, t, :], ninth[:, t, :], rest[:, t, :], TAKEN)
                last.then_inc(top_step, 1)
                dve.wait_ge(top_step, 5 * u + 4)
                dve.wait_ge(w_exp, u + 1)
                for t in range(NT):
                    last = stt(w[:, t, :], rest[:, t, :], TAKEN, w[:, t, :], ALU.is_equal, ALU.mult,
                               accum_out=w_sum[:, t:t + 1])
                last.then_inc(top_step, 1)
                dve.wait_ge(top_step, 5 * u + 5)
                nc.vector.reciprocal(w_inv[:, :], w_sum[:, :]).then_inc(w_summed, 1)

            def gate_h(g, j):
                lo, hi = GROUPS[g][0] // RANK, min(GROUPS[g][1], KR_ALL) // RANK
                dve.wait_ge(h_mm, 3 * j + 3 - g)
                tt(act_in[:, lo * RANK:hi * RANK].rearrange("p (e r) -> p e r", r=RANK),
                   P_H[g][:, 0:(hi - lo) * RANK].rearrange("p (e r) -> p e r", r=RANK),
                   gate[:, lo:hi].unsqueeze(2).broadcast_to([L, hi - lo, RANK]), ALU.mult).then_inc(gated, 1)

            def gates(j):
                at = GROUPS[2][1] - GROUPS[2][0] - EXPERTS
                score = P_H[2][:, at:at + EXPERTS]
                alone(dve, h_mm, 3 * j + 1)
                nc.vector.max(g8a[:, :], score).then_inc(gate_step, 1)
                dve.wait_ge(gate_step, 6 * j + 1)
                nc.vector.tensor_scalar(g_neg[:, :], g8a[:, 0:1], -1.0, None, ALU.mult)
                nc.vector.match_replace(g_rest[:, :], g8a[:, :], score, TAKEN).then_inc(gates_marked, 1)
                alone(dve, gates_marked, j + 1)
                nc.vector.max(g8b[:, :], g_rest[:, :]).then_inc(gate_step, 1)
                alone(dve, gate_step, 6 * j + 2)
                nc.vector.match_replace(g_mark[:, :], g8b[:, :], g_rest[:, :], TAKEN).then_inc(gate_step, 1)
                dve.wait_ge(gate_step, 6 * j + 3)
                dve.wait_ge(gate_exp, j + 1)
                stt(gate[:, :], g_mark[:, :], TAKEN, g_exp[:, :], ALU.is_equal, ALU.mult, accum_out=g_sum[:, :])\
                    .then_inc(gate_step, 1)
                dve.wait_ge(gate_step, 6 * j + 4)
                nc.vector.reciprocal(g_inv[:, :], g_sum[:, :]).then_inc(gate_step, 1)
                dve.wait_ge(gate_step, 6 * j + 5)
                nc.vector.tensor_scalar(out_scale[:, :], g_inv[:, :], SCALING, None, ALU.mult).then_inc(gate_step, 1)

            def stage_lo(n):
                _, hi, lo = jobs[n]
                dve.wait_ge(hi_staged, n + 1)
                tt(lo, staged(n), hi.bitcast(fp32), ALU.subtract).then_inc(lo_staged, 1)

            dve.wait_ge(const_in, 32)
            dve.wait_ge(zeroed, 1)
            dve.wait_ge(x_in[0], 16)
            statistics(xa[:, 0, :], 0, 0, ln1_step, mv1)

            def body(m, k, att, back, ffn, more):
                i = 2 * m + k
                j = i - 2
                for s in range(2):
                    u = 2 * i + s
                    v = u - 1
                    prev = back if s == 0 else att
                    if ffn:
                        for h in range(2):
                            dve.wait_ge(t_hi, 4 * j + 2 * s + h + 1)
                            half = slice(4 * h, 4 * h + 4)
                            tt(t_op[1][:, half, :].rearrange("p c l -> p (c l)"), P_T[h][:, :],
                               t_op[0][:, half, :].rearrange("p c l -> p (c l)").bitcast(fp32), ALU.subtract)\
                                .then_inc(t_lo, 1)
                    if prev:
                        dve.wait_ge(wt_hi, v + 1)
                        tt(wt_op[1][:, :], P_WT[:, :], wt_op[0][:, :].bitcast(fp32), ALU.subtract).then_inc(wt_lo, 1)
                    if s == 1 and back:
                        dve.wait_ge(x2, 2 * i)
                        dve.wait_ge(half_kept, i)
                        after(dve, ln2, i - 1)
                        statistics(res[:, 1 - k, :], 1, i - 1, ln2_step, mv2)
                    if att:
                        dve.wait_ge(q_swapped, 32 * (u + 1))
                        dve.wait_ge(ke_doubled, 32 * (u + 1))
                        tt(qf[:, :], qf[:, :], ke_r[:, s, :], ALU.mult).then_inc(real_term, 1)
                        dve.wait_ge(real_term, u + 1)
                        dve.wait_ge(q_terms, u + 1)
                        stt(qf[:, :], qs[:, :], sign[:, :], qf[:, :], ALU.mult, ALU.add).then_inc(zc, 1)
                    if prev:
                        dve.wait_ge(we_swapped, 32 * (v + 1))
                        tt(we[:, :], we[:, :], ke_r[:, 1 - s, :], ALU.mult)
                        dve.wait_ge(wo_swapped, 32 * (v + 1))
                        dve.wait_ge(ko_doubled, 32 * (v + 1))
                        tt(wo[:, :], wo[:, :], ko_r[:, :], ALU.mult).then_inc(real_terms, 1)
                    if ffn and s == 0:
                        gates(j)
                        gate_h(2, j)
                    if s == 1 and more:
                        dve.wait_ge(x_in[1 - k], 16 * (m + k + 1))
                        dve.wait_ge(ln1, i + 1)
                        statistics(xa[:, 1 - k, :], 0, i + 1, ln1_step, mv1)
                    if prev:
                        dve.wait_ge(real_terms, v + 1)
                        dve.wait_ge(e_terms, v + 1)
                        stt(we[:, :], we_s[:, :], sign[:, :], we[:, :], ALU.mult, ALU.add).then_inc(ze, 1)
                        dve.wait_ge(o_terms, v + 1)
                        stt(wo[:, :], wo_s[:, :], sign[:, :], wo[:, :], ALU.mult, ALU.add).then_inc(zo, 1)
                    if att:
                        choose_delays(u, P_CORR)
                    if ffn and s == 0:
                        gate_h(1, j)
                        gate_h(0, j)
                    if ffn and s == 1:
                        for h in range(2):
                            dve.wait_ge(y_mm, 2 * j + h + 1)
                            if h == 0:
                                dve.wait_ge(gate_step, 6 * j + 6)
                            half = res[:, k, h * 512:(h + 1) * 512]
                            stt(half, P_Y[h][:, :], out_scale[:, :], half, ALU.mult, ALU.add).then_inc(result, 1)
                    if isinstance(m, int) and i < 2:
                        for n in jobs_of(i, s):
                            stage_lo(n)
                    if prev:
                        dve.wait_ge(out_mm, v + 1)
                        if s == 1:
                            half = xa[:, k, 0:CH]
                            tt(half, half, P_OUT[:, :], ALU.add).then_inc(x2, 1)
                        else:
                            after(dve, stored[1 - k], 16 * (m + k - 1))
                            tt(res[:, 1 - k, CH:], xa[:, 1 - k, CH:], P_OUT[:, :], ALU.add).then_inc(x2, 1)

            iterations(dve, body)


def kernel(x, ctx_4096, L0_ffn_A, L0_ffn_B, L0_ffn_Wr):
    import numpy as _np
    import concourse.bacc as _bacc
    from concourse import mybir as _mybir
    from concourse.bass_utils import run_bass_kernel_spmd as _run

    a = _np.asarray(L0_ffn_A)
    b = _np.asarray(L0_ffn_B)
    plain_c, split_c, sign_c = constant_arrays()
    arrays = {
        "x": _np.ascontiguousarray(x),
        "ctx": _np.ascontiguousarray(ctx_4096),
        "a_t": _np.ascontiguousarray(a.reshape(KR_ALL, D).T),
        "wr_t": _np.ascontiguousarray(_np.asarray(L0_ffn_Wr).T),
        "b_t": _np.ascontiguousarray(b.transpose(0, 2, 1).reshape(KR_ALL, D)),
        "plain_c": plain_c, "split_c": split_c, "sign_c": sign_c,
    }
    nc = _bacc.Bacc("TRN2", target_bir_lowering=False, num_devices=1, dynamic_dma_scratch_size=1024)
    args = [nc.dram_tensor(n, v.shape, _mybir.dt.from_np(v.dtype), kind="ExternalInput").ap()
            for n, v in arrays.items()]
    args.append(nc.dram_tensor("out", (ROWS, L, D), _mybir.dt.float32, kind="ExternalOutput").ap())
    build(nc, *args)
    r = _run(nc, [arrays], core_ids=[0])
    return r.results[0]["out"]
```

```python
import concourse.bass as bass
from concourse import mybir
from contextlib import ExitStack
import numpy as np

L = 128
D = 1024
ROWS = 32
CH = 512
NT = CH // L
HALF = L // 2
TOPK = int(2 * np.log(L))
assert TOPK == 9
EXPERTS, RANK, CHOSEN = 64, 16, 16
KR_ALL = EXPERTS * RANK
SCALING = 32.0 / RANK
NC = D // L
AWC = KR_ALL + EXPERTS
GROUPS = ((0, 512), (512, 800), (800, AWC))
LN_EPS = 1e-5
TAKEN = -3.0e38

PLAIN = ("ident", "corr_inv")
SPLIT = ("even_fwd", "even_fwd_v", "odd_fwd", "odd_fwd_v", "even_inv", "odd_inv")


def constant_matrices():
    t = np.arange(L)
    k = np.arange(1, HALF)
    even = np.zeros((L, L))
    even[:, 0] = np.where(t % 2 == 0, 2.0, 0.0)
    even[:, 1:HALF] = np.cos(2 * np.pi * np.outer(t, k) / L)
    even[:, HALF] = np.where(t % 2 == 0, 0.0, 2.0)
    even[:, HALF + 1:] = -np.sin(2 * np.pi * np.outer(t, k) / L)
    even_v = even.copy()
    even_v[L - 1, [0, HALF]] += L
    theta = np.pi * (2 * np.arange(HALF) + 1) / L
    odd = np.concatenate([np.cos(np.outer(t, theta)), -np.sin(np.outer(t, theta))], 1)
    odd_v = odd.copy()
    odd_v[L - 1] -= odd.sum(0)
    inv = even.T * (2.0 / L)
    inv[0] /= 8
    inv[HALF] /= 8
    even_inv = inv / 2
    even_inv[HALF + 1:] *= -1
    odd_inv = odd.T / L
    odd_inv[HALF:] *= -1
    return dict(ident=np.eye(L), corr_inv=inv, even_fwd=even, even_fwd_v=even_v, odd_fwd=odd,
                odd_fwd_v=odd_v, even_inv=even_inv, odd_inv=odd_inv)


def high_part(a):
    f, e = np.frexp(a)
    return np.ldexp(np.rint(np.ldexp(f, 12)), e - 12)


def constant_arrays():
    m = constant_matrices()
    plain = np.concatenate([m[n] for n in PLAIN], 1).astype(np.float32)
    parts = []
    for n in SPLIT:
        hi = high_part(m[n])
        parts += [hi, high_part(m[n] - hi)]
    sign = np.where(np.arange(L) <= HALF, 1.0, -1.0).astype(np.float32)[:, None]
    return plain, np.concatenate(parts, 1).astype(np.float32), sign


def build(nc: bass.Bass, x, ctx, a_t, wr_t, b_t, plain_c, split_c, sign_c, out):
    fp32 = mybir.dt.float32
    fp32r = mybir.dt.float32r
    ALU = mybir.AluOpType
    ACT = mybir.ActivationFunctionType

    stack = ExitStack()
    with stack:
        def sb(name, shape, dt=fp32):
            return stack.enter_context(nc.sbuf_tensor(name, shape, dt))

        def sem(name):
            return stack.enter_context(nc.semaphore(name))

        aw = [sb(f"aw_{p}", [L, NC, AWC], fp32r) for p in ("hi", "lo")]
        bt = [sb(f"bt_{p}", [L, NC, D], fp32r) for p in ("hi", "lo")]
        plain = sb("plain", [L, len(PLAIN), L])
        split = sb("split", [L, 2 * len(SPLIT), L], fp32r)
        sign = sb("sign", [L, 1])
        ident = plain[:, 0, :]
        corr_inv = plain[:, 1, :]

        def const(name):
            n = 2 * SPLIT.index(name)
            return split[:, n, :], split[:, n + 1, :]

        xa = sb("xa", [L, D])
        c32 = sb("c32", [L, 2, CH])
        c_op = [sb(f"c_{p}", [L, CH], fp32r) for p in ("hi", "lo")]
        q_op = [sb(f"q_{p}", [L, CH], fp32r) for p in ("hi", "lo")]
        zf = sb("zf", [L, CH])
        qs = sb("qs", [L, CH])
        ke_r = sb("ke_r", [L, 2, CH])
        ke_i = sb("ke_i", [L, 2, CH])
        ko_r = sb("ko_r", [L, CH])
        ko_i = sb("ko_i", [L, CH])
        rest = sb("rest", [L, NT, L])
        w = sb("w", [L, NT, L])
        wt_op = [sb(f"wt_{p}", [L, CH], fp32r) for p in ("hi", "lo")]
        ze_op = [sb(f"ze_{p}", [L, CH], fp32r) for p in ("hi", "lo")]
        zo_op = [sb(f"zo_{p}", [L, CH], fp32r) for p in ("hi", "lo")]
        we = sb("we", [L, CH])
        we_s = sb("we_s", [L, CH])
        wo = sb("wo", [L, CH])
        wo_s = sb("wo_s", [L, CH])
        res = sb("res", [L, 2, D])
        y = sb("y", [L, D])
        act_in = sb("act_in", [L, D])
        t_op = [sb(f"t_{p}", [L, NC, L], fp32r) for p in ("hi", "lo")]
        top8 = sb("top8", [L, NT, 8])
        neg_max = sb("neg_max", [L, NT])
        next8 = sb("next8", [L, NT, 8])
        ninth = sb("ninth", [L, NT, 8])
        w_sum = sb("w_sum", [L, NT])
        w_inv = sb("w_inv", [L, NT])
        stats = sb("stats", [L, 2, 2, 6])
        mv = sb("mv", [L, 2, 2])
        rstd = sb("rstd", [L, 2])
        shift = sb("shift", [L, 2])
        minus_half = sb("minus_half", [L, 1])
        g8a = sb("g8a", [L, 8])
        g8b = sb("g8b", [L, 8])
        g_neg = sb("g_neg", [L, 1])
        g_rest = sb("g_rest", [L, EXPERTS])
        g_mark = sb("g_mark", [L, EXPERTS])
        g_exp = sb("g_exp", [L, EXPERTS])
        gate = sb("gate", [L, EXPERTS])
        g_sum = sb("g_sum", [L, 1])
        g_inv = sb("g_inv", [L, 1])
        out_scale = sb("out_scale", [L, 1])

        bank = [stack.enter_context(nc.psum_tensor(f"bank{b}", [L, 512], fp32)) for b in range(8)]
        P_H = bank[0:3]
        P_Y = bank[0:2]
        P_T = bank[3:5]
        P_KO, P_WO = bank[3], bank[4]
        P_WT = P_WE = bank[5]
        P_Q = bank[6]
        P_OUT = (bank[0], bank[2])
        P_KE = P_CORR = bank[7]

        split_flat = split[:, :, :].rearrange("p n l -> p (n l)")
        const_stage = [we[:, :], wo[:, :], we_s[:, :]]
        assert len(const_stage) * CH == 2 * len(SPLIT) * L
        jobs = [(wr_t.rearrange("(c p) e -> p c e", p=L), aw[0][:, :, KR_ALL:], aw[1][:, :, KR_ALL:])]
        jobs += [(a_t[c * L:(c + 1) * L, n:n + CH], aw[0][:, c, n:n + CH], aw[1][:, c, n:n + CH])
                 for c in range(NC) for n in (0, CH)]
        AW_JOBS = len(jobs)
        jobs += [(b_t[c * L:(c + 1) * L, n:n + CH], bt[0][:, c, n:n + CH], bt[1][:, c, n:n + CH])
                 for n in (0, CH) for c in range(NC)]
        JOBS_AT = (3, 4, 4, 4, 3, 4, 3, 2, 0, 2, 2, 2, 0)
        assert sum(JOBS_AT) == len(jobs)
        EARLY = sum(JOBS_AT[:9])
        stage = [t[:, n:n + CH] for t in (y[:, :], res[:, 1, :], act_in[:, :]) for n in (0, CH)]
        buffer_of = [n % len(stage) if n < EARLY else n % 2 for n in range(len(jobs))]

        def turn(n):
            return buffer_of[:n + 1].count(buffer_of[n])

        def freed_by(n):
            return max((p for p in range(n) if buffer_of[p] == buffer_of[n]), default=None)

        def staged(n):
            v = stage[buffer_of[n]]
            return v.rearrange("p (c e) -> p c e", e=EXPERTS) if n == 0 else v

        def jobs_of(m, i, s, part):
            if not (isinstance(m, int) and i < 3):
                return range(0)
            n = 1 + 2 * (2 * i + s) + part
            return range(sum(JOBS_AT[:n]), sum(JOBS_AT[:n + 1]))

        const_in = sem("const_in")
        split_in = [sem(f"split_in{n}") for n in range(len(const_stage))]
        staged_in = [sem(f"staged_in{n}") for n in range(len(stage))]
        x_in = sem("x_in")
        res_in = [sem(f"res_in{p}") for p in range(2)]
        c_in = [sem(f"c_in{p}") for p in range(2)]
        stored = sem("stored")
        zeroed = sem("zeroed")
        q_lo, c_lo, q_terms, e_terms, o_terms = (sem(n) for n in ("q_lo", "c_lo", "q_terms", "e_terms", "o_terms"))
        ze, zo, ze_lo, zo_lo = (sem(n) for n in ("ze", "zo", "ze_lo", "zo_lo"))
        ln1, ln2, rstd1, rstd2 = (sem(n) for n in ("ln1", "ln2", "rstd1", "rstd2"))
        hi_staged = sem("hi_staged")
        q_out, q_hi, c_hi, wt_hi, q_swapped, ke_r_out, ke_i_out, ko_out = (
            sem(n) for n in ("q_out", "q_hi", "c_hi", "wt_hi", "q_swapped", "ke_r_out", "ke_i_out", "ko_out"))
        t_hi, we_swapped, wo_swapped, ze_hi, zo_hi, w_exp, ln_out, gate_exp = (
            sem(n) for n in ("t_hi", "we_swapped", "wo_swapped", "ze_hi", "zo_hi", "w_exp", "ln_out", "gate_exp"))
        split_ready = sem("split_ready")
        lo_staged = sem("lo_staged")
        mv1, mv2, wt_lo, t_lo, zc, marked8, w_ready, x2 = (
            sem(n) for n in ("mv1", "mv2", "wt_lo", "t_lo", "zc", "marked8", "w_ready", "x2"))
        q_real, e_real, o_real = sem("q_real"), sem("e_real"), sem("o_real")
        gates_marked, gated, result = (sem(n) for n in ("gates_marked", "gated", "result"))
        ln1_step, ln2_step, top_step, gate_step = (sem(n) for n in ("ln1_step", "ln2_step", "top_step", "gate_step"))
        wt_mm, q_mm, ke_mm, t_mm, we_mm, wo_mm, corr_mm, ko_mm, out_mm, h_mm, y_mm = (
            sem(n) for n in ("wt_mm", "q_mm", "ke_mm", "t_mm", "we_mm", "wo_mm", "corr_mm", "ko_mm", "out_mm",
                             "h_mm", "y_mm"))

        def after(eng, s, n):
            if not (isinstance(n, int) and n <= 0):
                eng.wait_ge(s, n)

        def alone(eng, s, n):
            if isinstance(n, int):
                eng.wait_ge(s, n)
                return
            with eng.register() as count:
                eng.reg_mov(count, n)
                n = eng.snap(count, min_val=1)
                eng.wait_ge(const_in, 32)
                eng.wait_ge(s, n)

        def iterations(eng, body):
            def peeled(i):
                body(i // 2, i % 2, i < ROWS, 1 <= i <= ROWS, i >= 2, i + 1 < ROWS)
            for i in range(4):
                peeled(i)
            with eng.Fori(2, ROWS // 2 - 1) as m:
                body(m, 0, True, True, True, True)
                body(m, 1, True, True, True, True)
            for i in range(ROWS - 2, ROWS + 2):
                peeled(i)

        block = stack.enter_context(nc.Block())

        @block.sync
        def _(sp):
            def stage_in(n):
                if freed_by(n) is not None:
                    sp.wait_ge(lo_staged, freed_by(n) + 1)
                sp.dma_start(staged(n), jobs[n][0]).then_inc(staged_in[buffer_of[n]], 16)

            def stage_in_after(done):
                for n in range(len(jobs)):
                    if freed_by(n) in done:
                        stage_in(n)

            def row_of(t, row):
                return t[bass.ds(row, 1), :, :].rearrange("a p d -> (a p) d")

            def load_c(row, s):
                sp.dma_start(c32[:, s, :], ctx[bass.ds(row, 1), :, s * CH:(s + 1) * CH]
                             .rearrange("a p d -> (a p) d")).then_inc(c_in[s], 16)

            sp.dma_start(xa[:, :], row_of(x, 0)).then_inc(x_in, 16)
            load_c(0, 0)
            for n, dst in enumerate(const_stage):
                sp.dma_start(dst, split_c[:, n * CH:(n + 1) * CH]).then_inc(split_in[n], 16)
            sp.dma_start(plain[:, :, :], plain_c.rearrange("p (n l) -> p n l", l=L)).then_inc(const_in, 16)
            sp.dma_start(sign[:, :], sign_c).then_inc(const_in, 16)
            load_c(0, 1)
            for n in range(len(stage)):
                stage_in(n)
            stage_in_after(range(JOBS_AT[0]))

            def body(m, k, att, back, ffn, more):
                i = 2 * m + k
                if isinstance(m, int):
                    next_row, last_row, done_row = i + 1, i - 1, i - 2
                else:
                    next_row, last_row, done_row = sp.snap(i + 1), sp.snap(i - 1), sp.snap(i - 2)
                for s in range(2):
                    u = 2 * i + s
                    if s == 0 and back:
                        after(sp, result, 2 * i - 4)
                        sp.dma_start(res[:, 1 - k, :], row_of(x, last_row)).then_inc(res_in[1 - k], 16)
                    if more:
                        sp.wait_ge(c_lo, u + 1)
                        load_c(next_row, s)
                    if s == 0 and more:
                        sp.wait_ge(q_lo, 2 * i + 2)
                        sp.dma_start(xa[:, :], row_of(x, next_row)).then_inc(x_in, 16)
                    stage_in_after(jobs_of(m, i, s, 0))
                    stage_in_after(jobs_of(m, i, s, 1))
                    if s == 1 and ffn:
                        sp.wait_ge(result, 2 * (i - 1))
                        sp.dma_start(row_of(out, done_row), y[:, :]).then_inc(stored, 16)
                if isinstance(m, int) and i == 1:
                    sp.wait_ge(lo_staged, EARLY)

            iterations(sp, body)
            sp.wait_ge(stored, 16 * ROWS)

        @block.tensor
        def _(pe):
            def three(dst, st, mv_, start, stop):
                nc.tensor.matmul(dst, st[0], mv_[0], start=start, stop=False)
                nc.tensor.matmul(dst, st[0], mv_[1], start=False, stop=False)
                return nc.tensor.matmul(dst, st[1], mv_[0], start=False, stop=stop)

            def pair(t):
                return t[0][:, :], t[1][:, :]

            def transposes():
                for h in range(2):
                    for c in range(NC // 2):
                        last = nc.tensor.transpose(P_T[h][:, c * L:(c + 1) * L],
                                                   act_in[:, (4 * h + c) * L:(4 * h + c + 1) * L], ident)
                    last.then_inc(t_mm, 1)

            def h_group(g, j):
                lo, hi = GROUPS[g]
                for c in range(NC):
                    if g == 2 and c % 4 == 0:
                        pe.wait_ge(t_hi, 4 * j + c // 4 + 1)
                        pe.wait_ge(t_lo, 4 * j + c // 4 + 1)
                    last = three(P_H[g][:, 0:hi - lo], (t_op[0][:, c, :], t_op[1][:, c, :]),
                                 (aw[0][:, c, lo:hi], aw[1][:, c, lo:hi]), c == 0, c == NC - 1)
                last.then_inc(h_mm, 1)

            def y_half(h, j):
                for c in range(NC):
                    if h == 0 and c % 4 == 0:
                        pe.wait_ge(t_hi, 4 * j + c // 4 + 3)
                        pe.wait_ge(t_lo, 4 * j + c // 4 + 3)
                    last = three(P_Y[h][:, :], (t_op[0][:, c, :], t_op[1][:, c, :]),
                                 (bt[0][:, c, h * 512:(h + 1) * 512], bt[1][:, c, h * 512:(h + 1) * 512]),
                                 c == 0, c == NC - 1)
                last.then_inc(y_mm, 1)

            pe.wait_ge(const_in, 32)
            pe.wait_ge(split_ready, len(const_stage))

            def start_unit(u):
                pe.wait_ge(c_hi, u + 1)
                pe.wait_ge(c_lo, u + 1)
                after(pe, marked8, u)
                after(pe, w_exp, u)
                three(P_KE[:, :], const("even_fwd_v"), pair(c_op), True, True).then_inc(ke_mm, 1)
                pe.wait_ge(q_hi, u + 1)
                pe.wait_ge(q_lo, u + 1)
                after(pe, q_real, u)
                after(pe, q_swapped, u)
                three(P_Q[:, :], const("even_fwd"), pair(q_op), True, True).then_inc(q_mm, 1)

            start_unit(0)

            def body(m, k, att, back, ffn, more):
                i = 2 * m + k
                j = i - 2
                for s in range(2):
                    u = 2 * i + s
                    v = u - 1
                    z = u - 2
                    prev = back if s == 0 else att
                    if prev:
                        pe.wait_ge(w_ready, v + 1)
                        after(pe, e_real, v)
                        after(pe, we_swapped, v)
                        for t in range(NT):
                            last = nc.tensor.transpose(P_WT[:, t * L:(t + 1) * L], w[:, t, :], ident)
                        last.then_inc(wt_mm, 1)
                    if ffn:
                        if s == 0:
                            pe.wait_ge(ln_out, j + 1)
                        else:
                            pe.wait_ge(gated, 3 * (j + 1))
                        after(pe, ko_out, u if att else 2 * ROWS)
                        after(pe, o_real, v if prev else 2 * ROWS)
                        after(pe, wo_swapped, v if prev else 2 * ROWS)
                        transposes()
                    if back:
                        pe.wait_ge(ze_hi, z + 1)
                        pe.wait_ge(ze_lo, z + 1)
                        pe.wait_ge(zo_hi, z + 1)
                        pe.wait_ge(zo_lo, z + 1)
                        if s == 0:
                            after(pe, result, 2 * j)
                        if s == 1 and not ffn:
                            after(pe, x2, z - 1)
                        three(P_OUT[s][:, :], const("even_inv"), pair(ze_op), True, False)
                        three(P_OUT[s][:, :], const("odd_inv"), pair(zo_op), False, True).then_inc(out_mm, 1)
                    if prev:
                        pe.wait_ge(wt_hi, v + 1)
                        pe.wait_ge(wt_lo, v + 1)
                        three(P_WE[:, :], const("even_fwd"), pair(wt_op), True, True).then_inc(we_mm, 1)
                        if ffn:
                            pe.wait_ge(t_hi, 4 * j + 2 * s + 2)
                            pe.wait_ge(t_lo, 4 * j + 2 * s + 2)
                        else:
                            after(pe, o_real, v)
                            after(pe, wo_swapped, v)
                        three(P_WO[:, :], const("odd_fwd"), pair(wt_op), True, True).then_inc(wo_mm, 1)
                    if ffn and s == 0:
                        if isinstance(m, int) and i == 2:
                            pe.wait_ge(lo_staged, AW_JOBS)
                        after(pe, result, 2 * j)
                        pe.wait_ge(x2, 2 * i - 2 if back else 2 * ROWS)
                        h_group(2, j)
                        h_group(1, j)
                    if ffn and s == 1:
                        if isinstance(m, int) and i == 2:
                            pe.wait_ge(lo_staged, len(jobs) - NC)
                        y_half(0, j)
                    if att:
                        pe.wait_ge(zc, u + 1)
                        pe.wait_ge(ke_r_out, u + 1)
                        pe.wait_ge(ke_i_out, u + 1)
                        for t in range(NT):
                            last = nc.tensor.matmul(P_CORR[:, t * L:(t + 1) * L], zf[:, t * L:(t + 1) * L], corr_inv,
                                                    start=True, stop=True)
                        last.then_inc(corr_mm, 1)
                        if not ffn:
                            after(pe, ko_out, u)
                        three(P_KO[:, :], const("odd_fwd_v"), pair(c_op), True, True).then_inc(ko_mm, 1)
                    if ffn and s == 0:
                        pe.wait_ge(x2, 2 * i - 1 if back else 2 * ROWS)
                        h_group(0, j)
                    if ffn and s == 1:
                        if isinstance(m, int) and i == 2:
                            pe.wait_ge(lo_staged, len(jobs))
                        y_half(1, j)
                    if att and (s == 0 or more):
                        start_unit(u + 1)

            iterations(pe, body)

        @block.scalar
        def _(act):
            def copy(dst, src):
                return nc.scalar.activation(dst, src, ACT.Copy)

            def norm(dst, src, n):
                return nc.scalar.activation(dst, src, ACT.Identity, bias=shift[:, n:n + 1], scale=rstd[:, n:n + 1])

            def split_c_hi(u, s, i):
                act.wait_ge(c_in[s], 16 * (i + 1))
                after(act, ko_mm, u)
                copy(c_op[0][:, :], c32[:, s, :]).then_inc(c_hi, 1)

            def split_q_hi(u, s, i):
                act.wait_ge(ln1, i + 1)
                xs = xa[:, s * CH:(s + 1) * CH]
                norm(xs, xs, 0).then_inc(q_out, 1)
                act.wait_ge(q_out, u + 1)
                copy(q_op[0][:, :], xs).then_inc(q_hi, 1)

            def swapped(dst, src):
                copy(dst[0:HALF, :], src[HALF:L, :])
                return copy(dst[HALF:L, :], src[0:HALF, :])

            def stage_hi(n):
                act.wait_ge(staged_in[buffer_of[n]], 16 * turn(n))
                copy(jobs[n][1], staged(n)).then_inc(hi_staged, 1)

            split_c_hi(0, 0, 0)
            split_q_hi(0, 0, 0)
            for n in range(JOBS_AT[0]):
                stage_hi(n)

            def body(m, k, att, back, ffn, more):
                i = 2 * m + k
                j = i - 2
                for s in range(2):
                    u = 2 * i + s
                    v = u - 1
                    prev = back if s == 0 else att
                    if att:
                        act.wait_ge(ke_mm, u + 1)
                        after(act, e_real, u - 1)
                        copy(ke_r[0:HALF, s, :], P_KE[0:HALF, :])
                        copy(ke_r[HALF:L, s, :], P_KE[0:HALF, :]).then_inc(ke_r_out, 1)
                    if prev:
                        act.wait_ge(wt_mm, v + 1)
                        after(act, wo_mm, v)
                        copy(wt_op[0][:, :], P_WT[:, :]).then_inc(wt_hi, 1)
                    if ffn:
                        for h in range(2):
                            act.wait_ge(t_mm, 4 * j + 2 * s + h + 1)
                            if h == 0:
                                if s == 0:
                                    after(act, y_mm, 2 * j)
                                else:
                                    act.wait_ge(h_mm, 3 * (j + 1))
                            copy(t_op[0][:, 4 * h:4 * h + 4, :].rearrange("p c l -> p (c l)"), P_T[h][:, :])\
                                .then_inc(t_hi, 1)
                    if att:
                        act.wait_ge(q_mm, u + 1)
                        after(act, zc, u)
                        swapped(qs, P_Q).then_inc(q_swapped, 1)
                        after(act, e_terms, u - 1)
                        copy(ke_i[0:HALF, s, :], P_KE[HALF:L, :])
                        nc.scalar.activation(ke_i[HALF:L, s, :], P_KE[HALF:L, :], ACT.Copy, scale=sign[HALF:L, :])\
                            .then_inc(ke_i_out, 1)
                    if prev:
                        act.wait_ge(we_mm, v + 1)
                        after(act, ze, v)
                        swapped(we_s, P_WE).then_inc(we_swapped, 1)
                        act.wait_ge(wo_mm, v + 1)
                        after(act, zo, v)
                        swapped(wo_s, P_WO).then_inc(wo_swapped, 1)
                    if att and (s == 0 or more):
                        split_q_hi(u + 1, 1 - s, i + s)
                    for n in jobs_of(m, i, s, 0):
                        stage_hi(n)
                    if ffn and s == 0:
                        act.wait_ge(gates_marked, j + 1)
                        nc.scalar.activation(g_exp[:, :], P_H[2][:, GROUPS[2][1] - GROUPS[2][0] - EXPERTS:
                                                                 GROUPS[2][1] - GROUPS[2][0]],
                                             ACT.Exp, bias=g_neg[:, :]).then_inc(gate_exp, 1)
                    if prev:
                        act.wait_ge(ze, v + 1)
                        after(act, out_mm, v)
                        copy(ze_op[0][:, :], we[:, :]).then_inc(ze_hi, 1)
                        act.wait_ge(zo, v + 1)
                        copy(zo_op[0][:, :], wo[:, :]).then_inc(zo_hi, 1)
                    if att and (s == 0 or more):
                        split_c_hi(u + 1, 1 - s, i + s)
                    if att:
                        act.wait_ge(marked8, u + 1)
                        for t in range(NT):
                            last = nc.scalar.activation(w[:, t, :], P_CORR[:, t * L:(t + 1) * L], ACT.Exp,
                                                        bias=neg_max[:, t:t + 1])
                        last.then_inc(w_exp, 1)
                    if s == 1 and back:
                        if isinstance(m, int) and i == 1:
                            act.wait_ge(lo_staged, EARLY)
                        act.wait_ge(ln2, i)
                        after(act, t_mm, 4 * (j + 1))
                        norm(act_in[:, :], res[:, 1 - k, :], 1).then_inc(ln_out, 1)
                    if att:
                        act.wait_ge(ko_mm, u + 1)
                        after(act, o_real, u)
                        after(act, o_terms, u)
                        copy(ko_r[0:HALF, :], P_KO[0:HALF, :])
                        copy(ko_r[HALF:L, :], P_KO[0:HALF, :])
                        copy(ko_i[0:HALF, :], P_KO[HALF:L, :])
                        nc.scalar.mul(ko_i[HALF:L, :], P_KO[HALF:L, :], -1.0).then_inc(ko_out, 1)
                    for n in jobs_of(m, i, s, 1):
                        stage_hi(n)

            iterations(act, body)

        @block.gpsimd
        def _(pool):
            tt = nc.gpsimd.tensor_tensor
            nc.gpsimd.memset(minus_half[:, :], -0.5)
            nc.gpsimd.memset(ninth[:, :, :], TAKEN).then_inc(zeroed, 1)

            def split_c_lo(u, s):
                pool.wait_ge(c_hi, u + 1)
                tt(c_op[1][:, :], c32[:, s, :], c_op[0][:, :].bitcast(fp32), ALU.subtract).then_inc(c_lo, 1)

            def split_q_lo(u, s):
                pool.wait_ge(q_hi, u + 1)
                tt(q_op[1][:, :], xa[:, s * CH:(s + 1) * CH], q_op[0][:, :].bitcast(fp32), ALU.subtract)\
                    .then_inc(q_lo, 1)

            def scale_and_shift(n, row, ready, rooted, done):
                alone(pool, ready, row + 1)
                nc.gpsimd.tensor_scalar(rstd[:, n:n + 1], mv[:, n, 1:2], LN_EPS, 1.0, ALU.add, ALU.mult)\
                    .then_inc(rooted, 1)
                pool.wait_ge(rooted, 2 * row + 1)
                tt(rstd[:, n:n + 1], rstd[:, n:n + 1], minus_half[:, :], ALU.pow).then_inc(rooted, 1)
                alone(pool, rooted, 2 * row + 2)
                nc.gpsimd.tensor_scalar(shift[:, n:n + 1], mv[:, n, 0:1], -1.0, rstd[:, n:n + 1],
                                        ALU.mult, ALU.mult).then_inc(done, 1)

            scale_and_shift(0, 0, mv1, rstd1, ln1)
            split_c_lo(0, 0)
            split_q_lo(0, 0)

            def body(m, k, att, back, ffn, more):
                i = 2 * m + k
                j = i - 2
                for s in range(2):
                    u = 2 * i + s
                    v = u - 1
                    prev = back if s == 0 else att
                    if s == 1 and more:
                        scale_and_shift(0, i + 1, mv1, rstd1, ln1)
                    if att:
                        pool.wait_ge(q_swapped, u + 1)
                        pool.wait_ge(ke_i_out, u + 1)
                        tt(qs[:, :], qs[:, :], ke_i[:, s, :], ALU.mult).then_inc(q_terms, 1)
                    if prev:
                        pool.wait_ge(we_swapped, v + 1)
                        tt(we_s[:, :], we_s[:, :], ke_i[:, 1 - s, :], ALU.mult).then_inc(e_terms, 1)
                        pool.wait_ge(wo_swapped, v + 1)
                        pool.wait_ge(ko_out, v + 1)
                        tt(wo_s[:, :], wo_s[:, :], ko_i[:, :], ALU.mult).then_inc(o_terms, 1)
                    if prev:
                        pool.wait_ge(e_real, v + 1)
                        pool.wait_ge(e_terms, v + 1)
                        tt(we[:, :], we[:, :], we_s[:, :], ALU.add).then_inc(ze, 1)
                        pool.wait_ge(o_real, v + 1)
                        pool.wait_ge(o_terms, v + 1)
                        tt(wo[:, :], wo[:, :], wo_s[:, :], ALU.add).then_inc(zo, 1)
                    if s == 1 and back:
                        after(pool, ln_out, i - 1)
                        scale_and_shift(1, i - 1, mv2, rstd2, ln2)
                    if att and (s == 0 or more):
                        split_q_lo(u + 1, 1 - s)
                        split_c_lo(u + 1, 1 - s)
                    if prev:
                        pool.wait_ge(ze_hi, v + 1)
                        tt(ze_op[1][:, :], we[:, :], ze_op[0][:, :].bitcast(fp32), ALU.subtract).then_inc(ze_lo, 1)
                        pool.wait_ge(zo_hi, v + 1)
                        tt(zo_op[1][:, :], wo[:, :], zo_op[0][:, :].bitcast(fp32), ALU.subtract).then_inc(zo_lo, 1)

            iterations(pool, body)

        @block.vector
        def _(dve):
            tt = nc.vector.tensor_tensor
            stt = nc.vector.scalar_tensor_tensor

            def statistics(src, n, row, step, done):
                for h in range(2):
                    last = nc.vector.bn_stats(stats[:, n, h, :], src[:, h * 512:(h + 1) * 512])
                last.then_inc(step, 1)
                alone(dve, step, row + 1)
                nc.vector.bn_aggr(mv[:, n, :], stats[:, n, :, :]).then_inc(done, 1)

            def choose_delays(u, corr_):
                alone(dve, corr_mm, u + 1)
                for t in range(NT):
                    last = nc.vector.max(top8[:, t, :], corr_[:, t * L:(t + 1) * L])
                last.then_inc(top_step, 1)
                dve.wait_ge(top_step, 6 * u + 1)
                nc.vector.tensor_scalar(neg_max[:, :], top8[:, :, 0], -1.0, None, ALU.mult)
                for t in range(NT):
                    last = nc.vector.match_replace(rest[:, t, :], top8[:, t, :], corr_[:, t * L:(t + 1) * L], TAKEN)
                last.then_inc(marked8, 1)
                alone(dve, marked8, u + 1)
                for t in range(NT):
                    last = nc.vector.max(next8[:, t, :], rest[:, t, :])
                last.then_inc(top_step, 1)
                dve.wait_ge(top_step, 6 * u + 2)
                nc.vector.tensor_copy(ninth[:, :, 0], next8[:, :, 0]).then_inc(top_step, 1)
                alone(dve, top_step, 6 * u + 3)
                for t in range(NT):
                    last = nc.vector.match_replace(rest[:, t, :], ninth[:, t, :], rest[:, t, :], TAKEN)
                last.then_inc(top_step, 1)
                dve.wait_ge(top_step, 6 * u + 4)
                dve.wait_ge(w_exp, u + 1)
                for t in range(NT):
                    last = stt(w[:, t, :], rest[:, t, :], TAKEN, w[:, t, :], ALU.is_equal, ALU.mult,
                               accum_out=w_sum[:, t:t + 1])
                last.then_inc(top_step, 1)
                dve.wait_ge(top_step, 6 * u + 5)
                nc.vector.reciprocal(w_inv[:, :], w_sum[:, :]).then_inc(top_step, 1)
                dve.wait_ge(top_step, 6 * u + 6)
                tt(w[:, :, :], w[:, :, :], w_inv[:, :, None].broadcast_to([L, NT, L]), ALU.mult).then_inc(w_ready, 1)

            def gate_h(g, j):
                lo, hi = GROUPS[g][0] // RANK, min(GROUPS[g][1], KR_ALL) // RANK
                dve.wait_ge(h_mm, 3 * j + 3 - g)
                tt(act_in[:, lo * RANK:hi * RANK].rearrange("p (e r) -> p e r", r=RANK),
                   P_H[g][:, 0:(hi - lo) * RANK].rearrange("p (e r) -> p e r", r=RANK),
                   gate[:, lo:hi].unsqueeze(2).broadcast_to([L, hi - lo, RANK]), ALU.mult).then_inc(gated, 1)

            def gates(j):
                at = GROUPS[2][1] - GROUPS[2][0] - EXPERTS
                score = P_H[2][:, at:at + EXPERTS]
                alone(dve, h_mm, 3 * j + 1)
                nc.vector.max(g8a[:, :], score).then_inc(gate_step, 1)
                dve.wait_ge(gate_step, 6 * j + 1)
                nc.vector.tensor_scalar(g_neg[:, :], g8a[:, 0:1], -1.0, None, ALU.mult)
                nc.vector.match_replace(g_rest[:, :], g8a[:, :], score, TAKEN).then_inc(gates_marked, 1)
                alone(dve, gates_marked, j + 1)
                nc.vector.max(g8b[:, :], g_rest[:, :]).then_inc(gate_step, 1)
                alone(dve, gate_step, 6 * j + 2)
                nc.vector.match_replace(g_mark[:, :], g8b[:, :], g_rest[:, :], TAKEN).then_inc(gate_step, 1)
                dve.wait_ge(gate_step, 6 * j + 3)
                dve.wait_ge(gate_exp, j + 1)
                stt(gate[:, :], g_mark[:, :], TAKEN, g_exp[:, :], ALU.is_equal, ALU.mult, accum_out=g_sum[:, :])\
                    .then_inc(gate_step, 1)
                dve.wait_ge(gate_step, 6 * j + 4)
                nc.vector.reciprocal(g_inv[:, :], g_sum[:, :]).then_inc(gate_step, 1)
                dve.wait_ge(gate_step, 6 * j + 5)
                nc.vector.tensor_scalar(out_scale[:, :], g_inv[:, :], SCALING, None, ALU.mult).then_inc(gate_step, 1)

            def add_up(h, j, k):
                dve.wait_ge(y_mm, 2 * j + h + 1)
                if h == 0:
                    dve.wait_ge(gate_step, 6 * j + 6)
                    after(dve, stored, 16 * j)
                half = slice(h * 512, (h + 1) * 512)
                stt(y[:, half], P_Y[h][:, :], out_scale[:, :], res[:, k, half], ALU.mult, ALU.add).then_inc(result, 1)

            def stage_lo(n):
                _, hi, lo = jobs[n]
                dve.wait_ge(hi_staged, n + 1)
                tt(lo, staged(n), hi.bitcast(fp32), ALU.subtract).then_inc(lo_staged, 1)

            dve.wait_ge(x_in, 16)
            statistics(xa, 0, 0, ln1_step, mv1)
            for n, src in enumerate(const_stage):
                dve.wait_ge(split_in[n], 16)
                nc.vector.tensor_copy(split_flat[:, n * CH:(n + 1) * CH], src).then_inc(split_ready, 1)
            for n in range(JOBS_AT[0]):
                stage_lo(n)
            dve.wait_ge(zeroed, 1)

            def body(m, k, att, back, ffn, more):
                i = 2 * m + k
                j = i - 2
                for s in range(2):
                    u = 2 * i + s
                    v = u - 1
                    z = u - 2
                    prev = back if s == 0 else att
                    if s == 1 and more:
                        dve.wait_ge(x_in, 16 * (i + 2))
                        dve.wait_ge(ln1, i + 1)
                        statistics(xa, 0, i + 1, ln1_step, mv1)
                    if prev:
                        dve.wait_ge(wt_hi, v + 1)
                        tt(wt_op[1][:, :], P_WT[:, :], wt_op[0][:, :].bitcast(fp32), ALU.subtract).then_inc(wt_lo, 1)
                    if ffn:
                        for h in range(2):
                            dve.wait_ge(t_hi, 4 * j + 2 * s + h + 1)
                            half = slice(4 * h, 4 * h + 4)
                            tt(t_op[1][:, half, :].rearrange("p c l -> p (c l)"), P_T[h][:, :],
                               t_op[0][:, half, :].rearrange("p c l -> p (c l)").bitcast(fp32), ALU.subtract)\
                                .then_inc(t_lo, 1)
                    if att:
                        dve.wait_ge(ke_r_out, u + 1)
                        dve.wait_ge(q_swapped, u + 1)
                        tt(zf[:, :], P_Q[:, :], ke_r[:, s, :], ALU.mult).then_inc(q_real, 1)
                    if prev:
                        after(dve, ze_lo, v)
                        dve.wait_ge(we_swapped, v + 1)
                        tt(we[:, :], P_WE[:, :], ke_r[:, 1 - s, :], ALU.mult).then_inc(e_real, 1)
                        after(dve, zo_lo, v)
                        dve.wait_ge(wo_swapped, v + 1)
                        dve.wait_ge(ko_out, v + 1)
                        tt(wo[:, :], P_WO[:, :], ko_r[:, :], ALU.mult).then_inc(o_real, 1)
                    if back:
                        dve.wait_ge(out_mm, z + 1)
                        dve.wait_ge(res_in[1 - k], 16 * (m + k))
                        half = res[:, 1 - k, s * CH:(s + 1) * CH]
                        tt(half, half, P_OUT[s][:, :], ALU.add).then_inc(x2, 1)
                    if att:
                        dve.wait_ge(q_real, u + 1)
                        dve.wait_ge(q_terms, u + 1)
                        tt(zf[:, :], zf[:, :], qs[:, :], ALU.add).then_inc(zc, 1)
                    for n in jobs_of(m, i, s, 0):
                        stage_lo(n)
                    if s == 1 and back:
                        dve.wait_ge(x2, 2 * i)
                        after(dve, ln2, i - 1)
                        statistics(res[:, 1 - k, :], 1, i - 1, ln2_step, mv2)
                    if ffn and s == 0:
                        gates(j)
                        gate_h(2, j)
                    if ffn and s == 0:
                        gate_h(1, j)
                    if att:
                        choose_delays(u, P_CORR)
                    if ffn and s == 0:
                        gate_h(0, j)
                    if ffn and s == 1:
                        add_up(0, j, k)
                        add_up(1, j, k)
                    for n in jobs_of(m, i, s, 1):
                        stage_lo(n)

            iterations(dve, body)


def kernel(x, ctx_4096, L0_ffn_A, L0_ffn_B, L0_ffn_Wr):
    import numpy as _np
    import concourse.bacc as _bacc
    from concourse import mybir as _mybir
    from concourse.bass_utils import run_bass_kernel_spmd as _run

    a = _np.asarray(L0_ffn_A)
    b = _np.asarray(L0_ffn_B)
    plain_c, split_c, sign_c = constant_arrays()
    arrays = {
        "x": _np.ascontiguousarray(x),
        "ctx": _np.ascontiguousarray(ctx_4096),
        "a_t": _np.ascontiguousarray(a.reshape(KR_ALL, D).T),
        "wr_t": _np.ascontiguousarray(_np.asarray(L0_ffn_Wr).T),
        "b_t": _np.ascontiguousarray(b.transpose(0, 2, 1).reshape(KR_ALL, D)),
        "plain_c": plain_c, "split_c": split_c, "sign_c": sign_c,
    }
    nc = _bacc.Bacc("TRN2", target_bir_lowering=False, num_devices=1, dynamic_dma_scratch_size=1024)
    args = [nc.dram_tensor(n, v.shape, _mybir.dt.from_np(v.dtype), kind="ExternalInput").ap()
            for n, v in arrays.items()]
    args.append(nc.dram_tensor("out", (ROWS, L, D), _mybir.dt.float32, kind="ExternalOutput").ap())
    build(nc, *args)
    r = _run(nc, [arrays], core_ids=[0])
    return r.results[0]["out"]
```
